# Optimizing a Trainium2 kernel written in Bass

```python
import numpy as np
import jax
import jax.numpy as jnp

def _softmax(x, axis=-1):
    return jax.nn.softmax(x, axis=axis)

def _gelu(x):
    return jax.nn.gelu(x, approximate=True)

def _silu(x):
    return jax.nn.silu(x)

def _sigmoid(x):
    return jax.nn.sigmoid(x)

def _layernorm(x, axis=-1, eps=1e-05):
    m = jnp.mean(x, axis=axis, keepdims=True)
    v = jnp.var(x, axis=axis, keepdims=True)
    return (x - m) / jnp.sqrt(v + eps)

def _scatter_add(tgt, idx, src, axis=0):
    return tgt.at[idx].add(src)

def _segment_sum(src, seg, n):
    return jax.ops.segment_sum(src, seg, n)
kernel_name = 'mk_seq_postln_d2_jaxref_r4_af6795'

def setup_inputs(seed: int=0):
    np.random.seed(seed)
    _w = jnp.asarray

    def _L0_attn_setup():
        import jax, jax.numpy as jnp
        import numpy as np
        from jax import lax
        D_MODEL = 256
        D_STATE = 16
        D_CONV = 4
        EXPAND = 2
        D_INNER = D_MODEL * EXPAND
        B, L = (2, 256)
        EPS = 1e-05

        def _mamba_fwd(x, ln_g, ln_b, W_in, conv_w, conv_b, W_b, W_c, W_delta, b_delta, log_A, Dp, W_out):
            residual = x
            mu = jnp.mean(x, axis=-1, keepdims=True)
            var = jnp.var(x, axis=-1, keepdims=True)
            xn = (x - mu) * lax.rsqrt(var + EPS) * ln_g + ln_b
            xz = xn @ W_in
            x_br, z = jnp.split(xz, 2, axis=-1)
            xc = jnp.transpose(x_br, (0, 2, 1))
            xc = lax.conv_general_dilated(xc, conv_w, window_strides=(1,), padding=[(D_CONV - 1, 0)], feature_group_count=D_INNER, dimension_numbers=('NCH', 'OIH', 'NCH'))
            xc = xc + conv_b[None, :, None]
            xb = jax.nn.silu(jnp.transpose(xc, (0, 2, 1)))
            Bm = xb @ W_b
            Cm = xb @ W_c
            delta = jax.nn.softplus(xb @ W_delta + b_delta)
            A = -jnp.exp(log_A)
            A_bar = jnp.exp(delta[..., None] * A)
            Bx = delta[..., None] * Bm[:, :, None, :] * xb[..., None]

            def step(h, inp):
                a_t, bx_t, c_t = inp
                h = a_t * h + bx_t
                y_t = jnp.sum(h * c_t[:, None, :], axis=-1)
                return (h, y_t)
            h0 = jnp.zeros((xb.shape[0], D_INNER, D_STATE), xb.dtype)
            _, ys = lax.scan(step, h0, (jnp.swapaxes(A_bar, 0, 1), jnp.swapaxes(Bx, 0, 1), jnp.swapaxes(Cm, 0, 1)))
            y = jnp.swapaxes(ys, 0, 1)
            y = y + xb * Dp
            out = y * jax.nn.silu(z) @ W_out
            return out + residual
        key = jax.random.key(seed)
        ks = jax.random.split(key, 12)
        s = lambda fan_in: 1.0 / np.sqrt(fan_in)
        inp = {'x': jax.random.normal(ks[0], (B, L, D_MODEL), jnp.float32), 'ln_g': jnp.ones((D_MODEL,), jnp.float32), 'ln_b': jnp.zeros((D_MODEL,), jnp.float32), 'W_in': jax.random.normal(ks[1], (D_MODEL, 2 * D_INNER), jnp.float32) * s(D_MODEL), 'conv_w': jax.random.normal(ks[2], (D_INNER, 1, D_CONV), jnp.float32) * s(D_CONV), 'conv_b': jnp.zeros((D_INNER,), jnp.float32), 'W_b': jax.random.normal(ks[3], (D_INNER, D_STATE), jnp.float32) * s(D_INNER), 'W_c': jax.random.normal(ks[4], (D_INNER, D_STATE), jnp.float32) * s(D_INNER), 'W_delta': jax.random.normal(ks[5], (D_INNER, D_INNER), jnp.float32) * s(D_INNER), 'b_delta': jnp.zeros((D_INNER,), jnp.float32), 'log_A': jnp.broadcast_to(jnp.log(jnp.arange(1, D_STATE + 1, dtype=jnp.float32))[None, :], (D_INNER, D_STATE)).copy(), 'Dp': jnp.ones((D_INNER,), jnp.float32), 'W_out': jax.random.normal(ks[6], (D_INNER, D_MODEL), jnp.float32) * s(D_INNER)}
        return inp
    _L0_attn_in = _L0_attn_setup()

    def _L0_ffn_setup():
        import jax, jax.numpy as jnp
        import numpy as np
        key = jax.random.key(seed)
        ks = jax.random.split(key, 6)
        B, L, D, E = (4, 512, 256, 4)
        H = 4 * D
        x = jax.random.normal(ks[0], (B, L, D), dtype=jnp.float32)
        rW1 = jax.random.normal(ks[1], (D, 2 * D), dtype=jnp.float32) * (2.0 / D) ** 0.5
        rb1 = jnp.zeros((2 * D,), dtype=jnp.float32)
        rW2 = jax.random.normal(ks[2], (2 * D, E), dtype=jnp.float32) * (2.0 / (2 * D)) ** 0.5
        rb2 = jnp.zeros((E,), dtype=jnp.float32)
        We1 = jax.random.normal(ks[3], (E, D, H), dtype=jnp.float32) * (2.0 / D) ** 0.5
        be1 = jnp.zeros((E, H), dtype=jnp.float32)
        We2 = jax.random.normal(ks[4], (E, H, D), dtype=jnp.float32) * (2.0 / H) ** 0.5
        be2 = jnp.zeros((E, D), dtype=jnp.float32)
        return {'x': x, 'rW1': rW1, 'rb1': rb1, 'rW2': rW2, 'rb2': rb2, 'We1': We1, 'be1': be1, 'We2': We2, 'be2': be2}
    _L0_ffn_in = _L0_ffn_setup()

    def _L1_attn_setup():
        import jax, jax.numpy as jnp
        import numpy as np
        B, T, D, H = (2, 512, 256, 16)
        HD = D // H
        key = jax.random.key(seed)
        ks = jax.random.split(key, 9)
        w = lambda k, shp: jax.random.normal(k, shp, jnp.float32) * 0.02
        return {'x': jax.random.normal(ks[0], (B, T, D), jnp.float32), 'Wq': w(ks[1], (D, D)), 'bq': jnp.zeros((D,), jnp.float32), 'Wk': w(ks[2], (D, D)), 'bk': jnp.zeros((D,), jnp.float32), 'Wv': w(ks[3], (D, D)), 'bv': jnp.zeros((D,), jnp.float32), 'Wo': w(ks[4], (D, D)), 'bo': jnp.zeros((D,), jnp.float32), 'Wqs': w(ks[5], (3, HD)), 'bqs': jnp.zeros((3,), jnp.float32), 'Wks': w(ks[6], (3, HD)), 'bks': jnp.zeros((3,), jnp.float32), 'Wvs': w(ks[7], (3, HD)), 'bvs': jnp.zeros((3,), jnp.float32), 'temp': jnp.float32(1.0)}
    _L1_attn_in = _L1_attn_setup()

    def _L1_ffn_setup():
        import jax, jax.numpy as jnp
        import numpy as np
        HIDDEN = 256
        INTER = 1024
        key = jax.random.key(seed)
        k1, k2, k3, k4, k5 = jax.random.split(key, 5)
        hidden_states = jax.random.normal(k1, (4, 512, HIDDEN), dtype=jnp.float32)
        W1 = jax.random.normal(k2, (HIDDEN, INTER), dtype=jnp.float32) * (1.0 / np.sqrt(HIDDEN))
        b1 = jax.random.normal(k3, (INTER,), dtype=jnp.float32) * 0.02
        W2 = jax.random.normal(k4, (INTER, HIDDEN), dtype=jnp.float32) * (1.0 / np.sqrt(INTER))
        b2 = jax.random.normal(k5, (HIDDEN,), dtype=jnp.float32) * 0.02
        return {'hidden_states': hidden_states, 'W1': W1, 'b1': b1, 'W2': W2, 'b2': b2}
    _L1_ffn_in = _L1_ffn_setup()
    _d = {'L0_attn_x': _L0_attn_in['x'], 'L0_attn_ln_g': _L0_attn_in['ln_g'], 'L0_attn_ln_b': _L0_attn_in['ln_b'], 'L0_attn_W_in': _L0_attn_in['W_in'], 'L0_attn_conv_w': _L0_attn_in['conv_w'], 'L0_attn_conv_b': _L0_attn_in['conv_b'], 'L0_attn_W_b': _L0_attn_in['W_b'], 'L0_attn_W_c': _L0_attn_in['W_c'], 'L0_attn_W_delta': _L0_attn_in['W_delta'], 'L0_attn_b_delta': _L0_attn_in['b_delta'], 'L0_attn_log_A': _L0_attn_in['log_A'], 'L0_attn_Dp': _L0_attn_in['Dp'], 'L0_attn_W_out': _L0_attn_in['W_out'], 'L0_ffn_rW1': _L0_ffn_in['rW1'], 'L0_ffn_rb1': _L0_ffn_in['rb1'], 'L0_ffn_rW2': _L0_ffn_in['rW2'], 'L0_ffn_rb2': _L0_ffn_in['rb2'], 'L0_ffn_We1': _L0_ffn_in['We1'], 'L0_ffn_be1': _L0_ffn_in['be1'], 'L0_ffn_We2': _L0_ffn_in['We2'], 'L0_ffn_be2': _L0_ffn_in['be2'], 'L1_attn_Wq': _L1_attn_in['Wq'], 'L1_attn_bq': _L1_attn_in['bq'], 'L1_attn_Wk': _L1_attn_in['Wk'], 'L1_attn_bk': _L1_attn_in['bk'], 'L1_attn_Wv': _L1_attn_in['Wv'], 'L1_attn_bv': _L1_attn_in['bv'], 'L1_attn_Wo': _L1_attn_in['Wo'], 'L1_attn_bo': _L1_attn_in['bo'], 'L1_attn_Wqs': _L1_attn_in['Wqs'], 'L1_attn_bqs': _L1_attn_in['bqs'], 'L1_attn_Wks': _L1_attn_in['Wks'], 'L1_attn_bks': _L1_attn_in['bks'], 'L1_attn_Wvs': _L1_attn_in['Wvs'], 'L1_attn_bvs': _L1_attn_in['bvs'], 'L1_attn_temp': _L1_attn_in['temp'], 'L1_ffn_W1': _L1_ffn_in['W1'], 'L1_ffn_b1': _L1_ffn_in['b1'], 'L1_ffn_W2': _L1_ffn_in['W2'], 'L1_ffn_b2': _L1_ffn_in['b2']}
    _x0 = _d['L0_attn_x']
    _d['L0_attn_x'] = jax.random.normal(jax.random.fold_in(jax.random.key(seed), 1), (2, 2048, 256), dtype=_x0.dtype)
    del _x0
    return _d

def reference(L0_attn_x, L0_attn_ln_g, L0_attn_ln_b, L0_attn_W_in, L0_attn_conv_w, L0_attn_conv_b, L0_attn_W_b, L0_attn_W_c, L0_attn_W_delta, L0_attn_b_delta, L0_attn_log_A, L0_attn_Dp, L0_attn_W_out, L0_ffn_rW1, L0_ffn_rb1, L0_ffn_rW2, L0_ffn_rb2, L0_ffn_We1, L0_ffn_be1, L0_ffn_We2, L0_ffn_be2, L1_attn_Wq, L1_attn_bq, L1_attn_Wk, L1_attn_bk, L1_attn_Wv, L1_attn_bv, L1_attn_Wo, L1_attn_bo, L1_attn_Wqs, L1_attn_bqs, L1_attn_Wks, L1_attn_bks, L1_attn_Wvs, L1_attn_bvs, L1_attn_temp, L1_ffn_W1, L1_ffn_b1, L1_ffn_W2, L1_ffn_b2):

    def _L0_attn_ref(x, ln_g, ln_b, W_in, conv_w, conv_b, W_b, W_c, W_delta, b_delta, log_A, Dp, W_out):
        import jax, jax.numpy as jnp
        import numpy as np
        from jax import lax
        D_MODEL = 256
        D_STATE = 16
        D_CONV = 4
        EXPAND = 2
        D_INNER = D_MODEL * EXPAND
        B, L = (2, 256)
        EPS = 1e-05

        def _mamba_fwd(x, ln_g, ln_b, W_in, conv_w, conv_b, W_b, W_c, W_delta, b_delta, log_A, Dp, W_out):
            residual = x
            mu = jnp.mean(x, axis=-1, keepdims=True)
            var = jnp.var(x, axis=-1, keepdims=True)
            xn = (x - mu) * lax.rsqrt(var + EPS) * ln_g + ln_b
            xz = xn @ W_in
            x_br, z = jnp.split(xz, 2, axis=-1)
            xc = jnp.transpose(x_br, (0, 2, 1))
            xc = lax.conv_general_dilated(xc, conv_w, window_strides=(1,), padding=[(D_CONV - 1, 0)], feature_group_count=D_INNER, dimension_numbers=('NCH', 'OIH', 'NCH'))
            xc = xc + conv_b[None, :, None]
            xb = jax.nn.silu(jnp.transpose(xc, (0, 2, 1)))
            Bm = xb @ W_b
            Cm = xb @ W_c
            delta = jax.nn.softplus(xb @ W_delta + b_delta)
            A = -jnp.exp(log_A)
            A_bar = jnp.exp(delta[..., None] * A)
            Bx = delta[..., None] * Bm[:, :, None, :] * xb[..., None]

            def step(h, inp):
                a_t, bx_t, c_t = inp
                h = a_t * h + bx_t
                y_t = jnp.sum(h * c_t[:, None, :], axis=-1)
                return (h, y_t)
            h0 = jnp.zeros((xb.shape[0], D_INNER, D_STATE), xb.dtype)
            _, ys = lax.scan(step, h0, (jnp.swapaxes(A_bar, 0, 1), jnp.swapaxes(Bx, 0, 1), jnp.swapaxes(Cm, 0, 1)))
            y = jnp.swapaxes(ys, 0, 1)
            y = y + xb * Dp
            out = y * jax.nn.silu(z) @ W_out
            return out + residual
        return _mamba_fwd(x, ln_g, ln_b, W_in, conv_w, conv_b, W_b, W_c, W_delta, b_delta, log_A, Dp, W_out)

    def _L0_ffn_ref(x, rW1, rb1, rW2, rb2, We1, be1, We2, be2):
        import jax, jax.numpy as jnp
        import numpy as np
        E = We1.shape[0]
        top_k = min(2, E)
        rh = jax.nn.gelu(x @ rW1 + rb1, approximate=False)
        router_logits = rh @ rW2 + rb2
        router_probs = jax.nn.softmax(router_logits, axis=-1)
        expert_weights, expert_indices = jax.lax.top_k(router_probs, top_k)
        one_hot = jax.nn.one_hot(expert_indices, E, dtype=x.dtype)
        token_mask = one_hot.sum(axis=2)
        combine_w = (one_hot * expert_weights[..., None]).sum(axis=2)
        out = jnp.zeros_like(x)
        for e in range(E):
            xi = x * token_mask[..., e:e + 1]
            h = jax.nn.gelu(xi @ We1[e] + be1[e], approximate=False)
            yo = h @ We2[e] + be2[e]
            out = out + yo * combine_w[..., e:e + 1]
        return out

    def _L1_attn_ref(x, Wq, bq, Wk, bk, Wv, bv, Wo, bo, Wqs, bqs, Wks, bks, Wvs, bvs, temp):
        import jax, jax.numpy as jnp
        import numpy as np
        B, T, D, H = (2, 512, 256, 16)
        HD = D // H
        Bx, Tx, Dx = x.shape
        split = lambda y: y.reshape(Bx, Tx, H, HD).transpose(0, 2, 1, 3)
        q = split(x @ Wq.T + bq)
        k = split(x @ Wk.T + bk)
        v = split(x @ Wv.T + bv)
        q_stp = q @ Wqs.T + bqs
        k3 = k @ Wks.T + bks
        v3 = v @ Wvs.T + bvs
        cross_kv = jnp.cross(k3, v3, axis=-1)
        scores = (jnp.einsum('bhqd,bhkd->bhqk', q, k) + jnp.einsum('bhqc,bhkc->bhqk', q_stp, cross_kv)) * temp
        attn = jax.nn.softmax(scores, axis=-1)
        out = jnp.einsum('bhqk,bhkd->bhqd', attn, v)
        out = out.transpose(0, 2, 1, 3).reshape(Bx, Tx, Dx)
        return out @ Wo.T + bo

    def _L1_ffn_ref(hidden_states, W1, b1, W2, b2):
        import jax, jax.numpy as jnp
        import numpy as np
        HIDDEN = 256
        INTER = 1024
        h = jax.nn.relu(jnp.einsum('bsh,hi->bsi', hidden_states, W1) + b1)
        return jnp.einsum('bsi,ih->bsh', h, W2) + b2
    x = L0_attn_x
    x = _layernorm(x + _L0_attn_ref(x, L0_attn_ln_g, L0_attn_ln_b, L0_attn_W_in, L0_attn_conv_w, L0_attn_conv_b, L0_attn_W_b, L0_attn_W_c, L0_attn_W_delta, L0_attn_b_delta, L0_attn_log_A, L0_attn_Dp, L0_attn_W_out), axis=-1)
    x = _layernorm(x + _L0_ffn_ref(x, L0_ffn_rW1, L0_ffn_rb1, L0_ffn_rW2, L0_ffn_rb2, L0_ffn_We1, L0_ffn_be1, L0_ffn_We2, L0_ffn_be2), axis=-1)
    x = _layernorm(x + _L1_attn_ref(x, L1_attn_Wq, L1_attn_bq, L1_attn_Wk, L1_attn_bk, L1_attn_Wv, L1_attn_bv, L1_attn_Wo, L1_attn_bo, L1_attn_Wqs, L1_attn_bqs, L1_attn_Wks, L1_attn_bks, L1_attn_Wvs, L1_attn_bvs, L1_attn_temp), axis=-1)
    x = _layernorm(x + _L1_ffn_ref(x, L1_ffn_W1, L1_ffn_b1, L1_ffn_W2, L1_ffn_b2), axis=-1)
    return x

_drawn_inputs = setup_inputs


def setup_inputs(seed=0):
    import zlib

    import numpy as np

    out = dict(_drawn_inputs(seed))
    spreads = {'L0_attn_ln_g': (1.0, 0.2),
     'L0_attn_ln_b': (0.0, 0.1),
     'L0_attn_conv_b': (0.0, 0.1),
     'L0_attn_b_delta': (0.0, 0.1),
     'L0_attn_Dp': (1.0, 0.2),
     'L0_ffn_rb1': (0.0, 0.1),
     'L0_ffn_rb2': (0.0, 0.1),
     'L0_ffn_be1': (0.0, 0.1),
     'L0_ffn_be2': (0.0, 0.1),
     'L1_attn_bq': (0.0, 0.8),
     'L1_attn_bk': (0.0, 2.0),
     'L1_attn_bv': (0.0, 0.1),
     'L1_attn_bo': (0.0, 0.1),
     'L1_attn_bqs': (0.0, 2.0),
     'L1_attn_bks': (0.0, 2.0),
     'L1_attn_bvs': (0.0, 0.8)}
    factors = {'L1_attn_Wq': 8.0,
     'L1_attn_Wk': 8.0,
     'L1_attn_Wqs': 8.0,
     'L1_attn_Wks': 8.0,
     'L1_attn_Wvs': 8.0,
     'L1_ffn_b1': 5.0,
     'L1_ffn_b2': 3.554}
    for name, (base, spread) in spreads.items():
        noise = np.random.default_rng([zlib.crc32(name.encode()), seed]).standard_normal(out[name].shape)
        drawn = base * np.exp(spread * noise) if base else spread * noise
        out[name] = jnp.asarray(drawn.astype(out[name].dtype))
    for name, factor in factors.items():
        out[name] = (out[name] * factor).astype(out[name].dtype)
    return out
```

```python
from contextlib import ExitStack

import numpy as np
import concourse.bass as bass
from concourse import mybir

F32 = mybir.dt.float32
BF16 = mybir.dt.bfloat16
I32 = mybir.dt.int32
ALU = mybir.AluOpType
ACT = mybir.ActivationFunctionType
AX = mybir.AxisListType

P = 128
B, L, D = 2, 2048, 256
TOK = B * L
CH = 512
NCH = TOK // CH
CB = L // CH
TT = CH // P
KD = D // P
DI = 2 * D
DB = DI // P
NS = 16
TAPS = 4
NE = 4
RB = 2 * D // P
HB = 4 * D // P
NH = 16
HD = D // NH
C3 = 3
CX = C3 * NH
EPS = 1e-5
LN_STEPS = 16
RSQRT_SEED = 0x5F3759DF


def at_least(engine, semaphore, value):
    if not (isinstance(value, int) and value <= 0):
        engine.wait_ge(semaphore, value)


def wait_alone(engine, passed, semaphore, value):
    at_least(engine, semaphore, value)
    engine.sem_inc(passed, 1)


def layer_norm(nc, dve, steps, c, src, dst, tmp, passed):
    done = [0]

    def step(last, alone=False):
        last.then_inc(steps, 1)
        done[0] += 1
        if alone:
            wait_alone(dve, passed, steps, c * LN_STEPS + done[0])
        else:
            dve.wait_ge(steps, c * LN_STEPS + done[0])

    stats, mv, ve, half, seed, r, t = tmp
    n = src.shape[1]
    for i in range(n):
        last = nc.vector.bn_stats(stats[:, i, :], src[:, i, :])
    step(last, alone=True)
    for i in range(n):
        last = nc.vector.bn_aggr(mv[:, i, :], stats[:, i, :])
    step(last)
    step(nc.vector.tensor_scalar(ve, mv[:, :, 1], EPS, None, ALU.add))
    step(nc.vector.tensor_scalar(half, ve, -0.5, None, ALU.mult))
    step(nc.vector.tensor_scalar(seed, ve.bitcast(I32), 1, None, ALU.logical_shift_right))
    step(nc.vector.tensor_scalar(r.bitcast(I32), seed, -1.0, float(RSQRT_SEED), ALU.mult, ALU.add))
    for _ in range(3):
        step(nc.vector.tensor_tensor(t, r, r, ALU.mult))
        step(nc.vector.tensor_tensor(t, t, half, ALU.mult))
        step(nc.vector.scalar_tensor_tensor(r, t, 1.5, r, ALU.add, ALU.mult))
    for i in range(n):
        last = nc.vector.tensor_scalar(dst[:, i, :], src[:, i, :], mv[:, i, 0:1], r[:, i:i + 1],
                                       ALU.subtract, ALU.mult)
    step(last)
    assert done[0] == LN_STEPS


def quarters(n):
    return [] if n == 0 else [n - 1] if n < NS - 1 else [n - 1, n]


def ln_buffers(sb, name):
    return (sb(name + "_stats", [P, TT, 6])[:], sb(name + "_mv", [P, TT, 2])[:],
            sb(name + "_ve", [P, TT])[:], sb(name + "_half", [P, TT])[:],
            sb(name + "_seed", [P, TT], I32)[:], sb(name + "_r", [P, TT])[:],
            sb(name + "_t", [P, TT])[:])


def mamba_moe_qkv(nc, a, scr, chunks=NCH):
    with ExitStack() as ctx:
        def sb(name, shape, dt=F32):
            return ctx.enter_context(nc.sbuf_tensor(name, shape, dt))

        def sem(name):
            return ctx.enter_context(nc.semaphore(name))

        ident = sb("ident", [P, P])
        part_rows = sb("part_rows", [3 * 2 * NS, 2 * NS])
        w_in = sb("w_in", [P, KD, 2 * DI])
        w_delta = sb("w_delta", [P, DB, DI])
        w_bc3 = sb("w_bc3", [P, DB, 3 * 2 * NS])
        w_out = sb("w_out", [P, DB, D])
        cols = sb("cols", [P, a["cols"].shape[1]])
        neg_a = sb("neg_a", [P, NS * DB])
        r_w1 = sb("r_w1", [P, KD, RB * P])
        r_w2 = sb("r_w2", [P, RB, NE])
        r_b2 = sb("r_b2", [P, NE])
        e_w1 = sb("e_w1", [P, NE, KD, HB * P])
        e_w2 = sb("e_w2", [P, NE, HB, D])
        e_b2 = sb("e_b2", [NE, D])
        wqkv = sb("wqkv", [P, 3, KD, D])
        wx = sb("wx", [P, 4, KD, CX])
        xcols = sb("xcols", [CX, 4])
        wqs = sb("wqs", [CX, D])
        bqs = sb("bqs", [CX, NH])
        temp = sb("temp", [P, 1])

        def col(name, i=0):
            k = COL_AT[name] + i
            return cols[:, k:k + 1]

        bx = sb("bx", [P, DB, CH])
        xn_tok = bx[:, 0:2, :].rearrange("p a (s n) -> p (a s) n", n=D)
        xnT = bx[:, 2:4, :]
        x_br = sb("x_br", [P, DB, CH + TAPS - 1])
        delta = x_br[:, :, 0:CH]
        halo = sb("halo", [P, DB, TAPS - 1])
        xb = sb("xb", [P, DB, CH])
        gate = sb("gate", [P, DB, CH])
        g = gate
        du = sb("du", [P, DB, CH])
        decay = sb("decay", [P, DB, CH])
        pre = decay
        h = sb("h", [P, 2, DB, CH])
        conv = h[:, 0]
        soft = h[:, 0]
        c_sb = sb("c_sb", [P, 2, CH])
        bc_rest = c_sb[0:6 * NS, 0, :]
        bc_mid = c_sb[0:6 * NS, 1, :].bitcast(BF16)[:, 0:CH]
        bc3 = sb("bc3", [6 * NS, CH], BF16)
        sel = sb("sel", [6 * NS, 2 * NS], BF16)
        diag_d = sb("diag_d", [P, DB, P])
        state = sb("state", [P, NS, DB])
        x1_tok = sb("x1_tok", [P, TT, D])
        x1T = sb("x1T", [P, KD, CH])
        lg = sb("lg", [P, TT, NE])
        lmax = sb("lmax", [P, TT])
        lexp = sb("lexp", [P, TT, NE])
        prob = sb("prob", [P, TT, NE])
        beats = sb("beats", [P, NE, TT, NE])
        rank = sb("rank", [P, TT, NE])
        cw = sb("cw", [P, TT, NE])
        cwT = sb("cwT", [NE, TT, P])
        hid = sb("hid", [P, HB, CH])
        rh = hid[:, 0:RB, :]
        x2T = x1T
        vT = hid[:, 0:2, :]
        kt = vT
        qk = hid[:, 2:6, :]
        v_tok = hid[:, 6:8, :].rearrange("p a (s n) -> p (a s) n", n=D)
        cr = x1T[0:CX]
        kb_f = cr[0:NH, 1, :]
        parts = sb("parts", [P, 3, KD, CH], BF16)
        kb_parts = sb("kb_parts", [NH, 3, CH], BF16)
        ln_tmp = ln_buffers(sb, "ln")

        ps = ctx.enter_context(nc.psum_tensor("ps1", [P, 8, CH], F32))

        names = """w_mamba w_moe setup_dve x_loaded residual_loaded ln0_steps xn_turned xnT_ready xbr_mm xbr_copied
            conv_steps halo_kept halo_put xb_ready z_mm gate_ready delta_mm bc_mm pre_ready soft_ready
            delta_ready du_ready bc_steps b_mm c_mm c_copied decay_ready bx_ready h_ready state_kept
            hc_ready y_mm g_ready out_mm r_ready ln1_steps x1_turned x1T_ready router_steps lexp_ready
            ln2_steps k_steps crossed kb_scaled kb_steps parts_steps x2_stored v_stored
            q_stored k_stored kb_stored neg_ready passed_sp passed_pe passed_dve passed_pool""".split()
        s = {n: sem(n) for n in names}
        side_full = [sem("side_full0"), sem("side_full1")]
        side_free = [sem("side_free0"), sem("side_free1")]

        use, n = {}, 0
        order = [("router", i) for i in range(RB)] + [("logits", 0)]
        for e in range(NE):
            order += [("up", e, i) for i in range(HB)] + [("down", e, i) for i in range(2)]
        at = 1 + RB + HB
        order[at:at] = [("cwT", i) for i in range(2)] + [("base", i) for i in range(2)]
        order += [("x2T", i) for i in range(2)] + [("vT", i) for i in range(2)]
        order += [("v_tok", i) for i in range(2)] + [("q", i) for i in range(2)]
        order += [("k", i) for i in range(2)] + [("cross", i) for i in range(4)]
        order += [("kadd", i) for i in range(2)] + [("kb", 0)]
        use = {key: i for i, key in enumerate(order)}
        per_bank = len(order) // 2
        assert len(order) % 2 == 0

        def bank(key):
            return ps[:, 6 + use[key] % 2, :]

        def wait_free(engine, c, key):
            q = use[key]
            at_least(engine, side_free[q % 2], c * per_bank + q // 2)

        def wait_full(engine, c, key):
            q = use[key]
            engine.wait_ge(side_full[q % 2], c * per_bank + q // 2 + 1)

        def wait_read(engine, c, key):
            q = use[key]
            engine.wait_ge(side_free[q % 2], c * per_bank + q // 2 + 1)

        def full(last, key):
            last.then_inc(side_full[use[key] % 2], 1)

        def read(last, key):
            last.then_inc(side_free[use[key] % 2], 1)

        block = ctx.enter_context(nc.Block())
        mamba_loads = [(ident, "ident"), (part_rows, "part_rows"), (cols, "cols"), (neg_a, "log_a"),
                       (w_in, "w_in"), (w_delta, "w_delta"), (w_bc3, "w_bc3"), (w_out, "w_out")]
        moe_loads = [(r_w1, "r_w1"), (r_w2, "r_w2"), (e_w1, "e_w1"), (e_w2, "e_w2"),
                     (wqkv, "wqkv"), (wx, "wx"), (xcols, "xcols"), (wqs, "wqs"), (bqs, "bqs"),
                     (e_b2, "e_b2")]
        moe_rows = [(r_b2[:], a["r_b2"]),
                    (temp[:], a["temp"])]
        W_MAMBA = 16 * len(mamba_loads)
        W_MOE = 16 * (len(moe_loads) + len(moe_rows))

        @block.sync
        def _(sp):
            def load_x(c):
                at_least(sp, s["h_ready"], c * NS * DB)
                sp.dma_start(xn_tok, a["x"][bass.ds(c * CH, CH), :].rearrange("(s p) n -> p s n", p=P))\
                    .then_inc(s["x_loaded"], 16)

            def load_residual(c):
                at_least(sp, s["x2_stored"], 16 * c)
                if not isinstance(c, int):
                    for k in range(KD):
                        wait_full(sp, c - 1, ("x2T", k))
                        sp.sem_inc(s["passed_sp"], 1)
                sp.dma_start(x1_tok[:], a["x"][bass.ds(c * CH, CH), :].rearrange("(s p) n -> p s n", p=P))\
                    .then_inc(s["residual_loaded"], 16)

            def store_x2(c):
                tok = bass.ds(c * CH, CH)
                sp.wait_ge(s["ln2_steps"], (c + 1) * LN_STEPS)
                sp.dma_start(scr["x2"][tok, :].rearrange("(s p) n -> p s n", p=P), x1_tok[:])\
                    .then_inc(s["x2_stored"], 16)

            def store(c):
                tok = bass.ds(c * CH, CH)
                for pair in range(2):
                    wait_read(sp, c, ("v_tok", pair))
                    sp.sem_inc(s["passed_sp"], 1)
                sp.dma_start(scr["v"][tok, :].rearrange("(s p) n -> p s n", p=P), v_tok)\
                    .then_inc(s["v_stored"], 16)
                for i, name in enumerate(("q", "k")):
                    wait_alone(sp, s["passed_sp"], s["parts_steps"], c * 8 + 4 * i + 4)
                    for m in range(KD):
                        rows = bass.ds((c // CB) * D + m * P, P)
                        sp.dma_start(scr[name][rows, bass.ds(c % CB, 1), :, :].rearrange("p o i t -> p (o i) t"),
                                     parts[:, :, m, :]).then_inc(s[name + "_stored"], 16)
                wait_alone(sp, s["passed_sp"], s["kb_steps"], c * 5 + 5)
                sp.dma_start(scr["kb"][bass.ds((c // CB) * NH, NH), bass.ds(c % CB, 1), :, :]
                             .rearrange("p o i t -> p (o i) t"), kb_parts[:]).then_inc(s["kb_stored"], 16)

            for t, name in mamba_loads[:4]:
                sp.dma_start(t[:], a[name]).then_inc(s["w_mamba"], 16)
            load_x(0)
            for t, name in mamba_loads[4:]:
                sp.dma_start(t[:], a[name]).then_inc(s["w_mamba"], 16)
            for t, name in moe_loads:
                sp.dma_start(t[:], a[name]).then_inc(s["w_moe"], 16)
            for t, src in moe_rows:
                sp.dma_start(t, src.partition_broadcast(P)).then_inc(s["w_moe"], 16)
            load_residual(0)
            with sp.Fori(1, chunks) as c:
                load_x(c)
                store_x2(c - 1)
                load_residual(c)
                store(c - 1)
            store_x2(chunks - 1)
            store(chunks - 1)
            for name, n in (("x2", 1), ("v", 1), ("q", 2), ("k", 2), ("kb", 1)):
                sp.wait_ge(s[name + "_stored"], 16 * n * chunks)

        @block.tensor
        def _(pe):
            mm = nc.tensor.matmul

            def front(c):
                at_least(pe, s["g_ready"], c)
                at_least(pe, s["x1T_ready"], c)
                pe.wait_ge(s["ln0_steps"], (c + 1) * LN_STEPS)
                for k in range(KD):
                    for i in range(TT):
                        last = nc.tensor.transpose(ps[:, k, i * P:(i + 1) * P],
                                                   xn_tok[:, i, k * P:(k + 1) * P], ident[:])
                last.then_inc(s["xn_turned"], 1)
                pe.wait_ge(s["xnT_ready"], c + 1)
                for e in range(DB):
                    for k in range(KD):
                        last = mm(ps[:, 2 + e, :], w_in[:, k, e * P:(e + 1) * P], xnT[:, k, :],
                                  start=k == 0, stop=k == KD - 1)
                    last.then_inc(s["xbr_mm"], 1)
                for e in range(DB):
                    if e >= 2:
                        pe.wait_ge(s["xbr_copied"], c * DB + e - 1)
                    for k in range(KD):
                        last = mm(ps[:, e, :], w_in[:, k, DI + e * P:DI + (e + 1) * P], xnT[:, k, :],
                                  start=k == 0, stop=k == KD - 1)
                    last.then_inc(s["z_mm"], 1)
                pe.wait_ge(s["xb_ready"], (c + 1) * DB)
                pe.wait_ge(s["xbr_copied"], (c + 1) * DB)
                for k in range(DB):
                    last = mm(ps[0:6 * NS, 4, :], w_bc3[:, k, :], xb[:, k, :],
                              start=k == 0, stop=k == DB - 1)
                last.then_inc(s["bc_mm"], 1)
                for m in range(DB):
                    pe.wait_ge(s["gate_ready"], c * DB + m + 1)
                    for k in range(DB):
                        last = mm(ps[:, m, :], w_delta[:, k, m * P:(m + 1) * P], xb[:, k, :],
                                  start=k == 0, stop=k == DB - 1)
                    last.then_inc(s["delta_mm"], 1)

            def broadcast(c, n):
                if n == 0:
                    pe.wait_ge(s["bc_steps"], c * 5 + 5)
                at_least(pe, s["bx_ready"], c * NS + n)
                mm(ps[:, 4, :], sel[:, n:n + 1].to_broadcast([6 * NS, P]), bc3[:], start=True, stop=True).then_inc(s["b_mm"], 1)
                at_least(pe, s["c_copied"], c * NS + n)
                mm(ps[:, 5, :], sel[:, NS + n:NS + n + 1].to_broadcast([6 * NS, P]), bc3[:], start=True, stop=True).then_inc(s["c_mm"], 1)

            def y_start(c):
                pe.wait_ge(s["pre_ready"], (c + 1) * DB)
                for m in range(DB):
                    mm(ps[:, m, :], diag_d[:, m, :], xb[:, m, :], start=True, stop=False)

            def y_add(c, n):
                pe.wait_ge(s["hc_ready"], c * NS + n + 1)
                for m in range(DB):
                    mm(ps[:, m, :], ident[:], h[:, n % 2, m, :], start=False, stop=n == NS - 1)\
                        .then_inc(s["y_mm"], 1)

            def project_out(c):
                pe.wait_ge(s["g_ready"], c + 1)
                pe.wait_ge(s["bx_ready"], (c + 1) * NS)
                pe.wait_ge(s["c_copied"], (c + 1) * NS)
                for i in range(TT):
                    o = ps[:, 4 + i // 2, (i % 2) * D:(i % 2 + 1) * D]
                    for m in range(DB):
                        last = mm(o, g[:, m, i * P:(i + 1) * P], w_out[:, m, :],
                                  start=m == 0, stop=m == DB - 1)
                last.then_inc(s["out_mm"], 1)

            def turn_x1(c):
                pe.wait_ge(s["ln1_steps"], (c + 1) * LN_STEPS)
                for k in range(KD):
                    for i in range(TT):
                        last = nc.tensor.transpose(ps[:, 4 + k, i * P:(i + 1) * P],
                                                   x1_tok[:, i, k * P:(k + 1) * P], ident[:])
                last.then_inc(s["x1_turned"], 1)

            def router(c):
                pe.wait_ge(s["x1T_ready"], c + 1)
                for i in range(RB):
                    wait_free(pe, c, ("router", i))
                    for k in range(KD):
                        last = mm(bank(("router", i)), r_w1[:, k, i * P:(i + 1) * P], x1T[:, k, :],
                                  start=k == 0, stop=k == KD - 1)
                    full(last, ("router", i))
                wait_free(pe, c, ("logits", 0))
                wait_read(pe, c, ("router", RB - 1))
                for i in range(TT):
                    for k in range(RB):
                        last = mm(bank(("logits", 0))[:, i * NE:(i + 1) * NE],
                                  rh[:, k, i * P:(i + 1) * P], r_w2[:, k, :],
                                  start=k == 0, stop=k == RB - 1)
                full(last, ("logits", 0))

            def base(c):
                pe.wait_ge(s["router_steps"], c * 8 + 8)
                for j in range(2):
                    wait_free(pe, c, ("cwT", j))
                    for i in range(2):
                        last = nc.tensor.transpose(bank(("cwT", j))[0:NE, i * P:(i + 1) * P],
                                                   cw[:, 2 * j + i, :], ident[:])
                    full(last, ("cwT", j))
                for j in range(2):
                    wait_free(pe, c, ("base", j))
                    wait_read(pe, c, ("cwT", j))
                    for i in range(2):
                        last = mm(bank(("base", j))[:, i * D:(i + 1) * D], cwT[:, 2 * j + i, :],
                                  e_b2[:], start=True, stop=True)
                    full(last, ("base", j))

            def up(c, e, blocks):
                for i in blocks:
                    key = ("up", e, i)
                    wait_free(pe, c, key)
                    for k in range(KD):
                        last = mm(bank(key), e_w1[:, e, k, i * P:(i + 1) * P], x1T[:, k, :],
                                  start=k == 0, stop=k == KD - 1)
                    full(last, key)

            def down(c, e, pair):
                wait_read(pe, c, ("up", e, HB - 2))
                wait_read(pe, c, ("up", e, HB - 1))
                key = ("down", e, pair)
                wait_free(pe, c, key)
                for i in range(2):
                    for k in range(HB):
                        last = mm(bank(key)[:, i * D:(i + 1) * D],
                                  hid[:, k, (2 * pair + i) * P:(2 * pair + i + 1) * P],
                                  e_w2[:, e, k, :], start=k == 0, stop=k == HB - 1)
                full(last, key)

            def experts(c, n):
                if n == 0:
                    router(c)
                for j in quarters(n):
                    e, part = j // 4, j % 4
                    if part < 2:
                        up(c, e, range(4 * part, 4 * part + 4))
                    else:
                        if j == 2:
                            base(c)
                        down(c, e, part - 2)

            def project(c, key, w, rhs, rows=P):
                wait_free(pe, c, key)
                for k in range(KD):
                    last = mm(bank(key)[0:rows], w[:, k, :], rhs[:, k, :],
                              start=k == 0, stop=k == KD - 1)
                full(last, key)

            def qkv(c):
                pe.wait_ge(s["ln2_steps"], (c + 1) * LN_STEPS)
                for k in range(KD):
                    wait_free(pe, c, ("x2T", k))
                    for i in range(TT):
                        last = nc.tensor.transpose(bank(("x2T", k))[:, i * P:(i + 1) * P],
                                                   x1_tok[:, i, k * P:(k + 1) * P], ident[:])
                    full(last, ("x2T", k))
                wait_read(pe, c, ("x2T", 0))
                wait_read(pe, c, ("x2T", 1))
                for m in range(KD):
                    project(c, ("vT", m), wqkv[:, 2, :, m * P:(m + 1) * P], x2T)
                for pair in range(2):
                    key = ("v_tok", pair)
                    wait_free(pe, c, key)
                    wait_read(pe, c, ("vT", 0))
                    wait_read(pe, c, ("vT", 1))
                    for i in range(2):
                        for m in range(KD):
                            t = (2 * pair + i) * P
                            last = nc.tensor.transpose(
                                bank(key)[:, i * D + m * P:i * D + (m + 1) * P],
                                vT[:, m, t:t + P], ident[:])
                    full(last, key)
                for m in range(KD):
                    project(c, ("q", m), wqkv[:, 0, :, m * P:(m + 1) * P], x2T)
                for m in range(KD):
                    project(c, ("k", m), wqkv[:, 1, :, m * P:(m + 1) * P], x2T)
                wait_read(pe, c, ("k", 0))
                wait_read(pe, c, ("k", 1))
                for i in range(4):
                    project(c, ("cross", i), wx[:, i], vT if i % 2 == 0 else qk[:, 2:4, :], CX)
                pe.wait_ge(s["crossed"], c + 1)
                for m in range(KD):
                    wait_free(pe, c, ("kadd", m))
                    full(mm(bank(("kadd", m)), wqs[:, m * P:(m + 1) * P], cr[:, 0, :],
                            start=True, stop=True), ("kadd", m))
                wait_free(pe, c, ("kb", 0))
                pe.sem_inc(s["passed_pe"], 1)
                full(mm(bank(("kb", 0))[0:NH], bqs[:], cr[:, 0, :], start=True, stop=True), ("kb", 0))

            pe.wait_ge(s["w_mamba"], W_MAMBA)
            pe.wait_ge(s["setup_dve"], 6)

            def chunk(c, before):
                front(c)
                y_start(c)
                broadcast(c, 0)
                broadcast(c, 1)
                for n in range(NS):
                    if n + 2 < NS:
                        broadcast(c, n + 2)
                    if before is not None:
                        experts(before, n)
                    y_add(c, n)
                project_out(c)
                if before is not None:
                    qkv(before)
                turn_x1(c)

            chunk(0, None)
            pe.wait_ge(s["w_moe"], W_MOE)
            with pe.Fori(1, chunks) as c:
                chunk(c, c - 1)
            for n in range(NS):
                experts(chunks - 1, n)
            qkv(chunks - 1)

        @block.scalar
        def _(act):
            fn = nc.scalar.activation

            def front(c):
                at_least(act, s["h_ready"], c * NS * DB)
                at_least(act, s["g_ready"], c)
                for e in range(DB):
                    act.wait_ge(s["xbr_mm"], c * DB + e + 1)
                    fn(x_br[:, e, TAPS - 1:], ps[:, 2 + e, :], ACT.Copy).then_inc(s["xbr_copied"], 1)
                for e in range(DB):
                    act.wait_ge(s["z_mm"], c * DB + e + 1)
                    fn(gate[:, e, :], ps[:, e, :], ACT.Silu).then_inc(s["gate_ready"], 1)
                for e in range(DB):
                    act.wait_ge(s["conv_steps"], c * DB * TAPS + (TAPS - 1) * DB + e + 1)
                    fn(xb[:, e, :], conv[:, e, :], ACT.Silu).then_inc(s["xb_ready"], 1)
                for i in range(2):
                    half = slice(2 * i, 2 * i + 2)
                    act.wait_ge(s["pre_ready"], c * DB + 2 * i + 2)
                    if i == 0:
                        act.wait_ge(s["xb_ready"], (c + 1) * DB)
                    fn(soft[:, half], pre[:, half], ACT.Abs).then_inc(s["soft_ready"], 1)
                    act.wait_ge(s["soft_ready"], c * 6 + 3 * i + 1)
                    fn(soft[:, half], soft[:, half], ACT.Exp, scale=-1.0).then_inc(s["soft_ready"], 1)
                    act.wait_ge(s["soft_ready"], c * 6 + 3 * i + 2)
                    fn(soft[:, half], soft[:, half], ACT.Ln, bias=1.0).then_inc(s["soft_ready"], 1)

            def copy_c(c, n):
                act.wait_ge(s["c_mm"], c * NS + n + 1)
                at_least(act, s["hc_ready"], c * NS + n - 1 if n else c * NS)
                fn(c_sb[:, n % 2, :], ps[:, 5, :], ACT.Copy).then_inc(s["c_copied"], 1)

            def decays(c, n):
                for m in range(DB):
                    if n == 0 and m == 0:
                        act.wait_ge(s["delta_ready"], (c + 1) * 2)
                    u = n * DB + m
                    at_least(act, s["h_ready"], c * NS * DB + u - 3 if u >= 4 else c * NS * DB)
                    fn(decay[:, m, :], delta[:, m, :], ACT.Exp,
                       scale=neg_a[:, n * DB + m:n * DB + m + 1]).then_inc(s["decay_ready"], 1)

            def back(c):
                act.wait_ge(s["x1_turned"], c + 1)
                at_least(act, s["kb_steps"], c * 5)
                fn(x1T[:], ps[:, 4:6, :], ACT.Copy).then_inc(s["x1T_ready"], 1)

            def gelu(c, key, dst, bias):
                wait_full(act, c, key)
                read(fn(dst, bank(key), ACT.Gelu, bias=bias), key)

            def experts(c, n):
                if n == 0:
                    at_least(act, s["v_stored"], 16 * c)
                    at_least(act, s["parts_steps"], 8 * c)
                    at_least(act, s["k_steps"], 4 * c)
                    for i in range(RB):
                        gelu(c, ("router", i), rh[:, i, :], col("r_b1", i))
                if n == 1:
                    act.wait_ge(s["router_steps"], c * 8 + 2)
                    fn(lexp[:], lg[:], ACT.Exp).then_inc(s["lexp_ready"], 1)
                for j in quarters(n):
                    e, part = j // 4, j % 4
                    if part < 2:
                        for i in range(4 * part, 4 * part + 4):
                            gelu(c, ("up", e, i), hid[:, i, :], col("e_b1", e * HB + i))

            def qkv(c):
                for k in range(KD):
                    wait_full(act, c, ("x2T", k))
                    read(fn(x2T[:, k, :], bank(("x2T", k)), ACT.Copy), ("x2T", k))
                for m in range(KD):
                    wait_full(act, c, ("vT", m))
                    read(fn(vT[:, m, :], bank(("vT", m)), ACT.Identity, bias=col("bv", m)), ("vT", m))
                for i in range(2):
                    wait_full(act, c, ("v_tok", i))
                    read(fn(v_tok[:, 2 * i:2 * i + 2, :].rearrange("p s n -> p (s n)"),
                            bank(("v_tok", i)), ACT.Copy), ("v_tok", i))
                for j, name in enumerate(("q", "k")):
                    for m in range(KD):
                        wait_full(act, c, (name, m))
                        read(fn(qk[:, 2 * j + m, :], bank((name, m)), ACT.Identity,
                                bias=col("b" + name, m)), (name, m))
                for i in (0, 2):
                    wait_full(act, c, ("cross", i))
                    read(fn(cr[:, i // 2, :], bank(("cross", i))[0:CX], ACT.Identity,
                            bias=xcols[:, i:i + 1]), ("cross", i))
                wait_full(act, c, ("kb", 0))
                at_least(act, s["kb_steps"], c * 5)
                read(fn(kb_f, bank(("kb", 0))[0:NH], ACT.Copy, scale=temp[0:NH, :]), ("kb", 0))

            act.wait_ge(s["w_mamba"], W_MAMBA)
            fn(neg_a[:], neg_a[:], ACT.Exp).then_inc(s["neg_ready"], 1)
            act.wait_ge(s["setup_dve"], 6)

            def chunk(c, before):
                front(c)
                copy_c(c, 0)
                for n in range(NS):
                    decays(c, n)
                    if n + 1 < NS:
                        copy_c(c, n + 1)
                    if before is not None:
                        experts(before, n)
                if before is not None:
                    qkv(before)
                back(c)

            chunk(0, None)
            act.wait_ge(s["w_moe"], W_MOE)
            with act.Fori(1, chunks) as c:
                chunk(c, c - 1)
            for n in range(NS):
                experts(chunks - 1, n)
            qkv(chunks - 1)

        @block.vector
        def _(dve):
            v = nc.vector

            def front(c):
                dve.wait_ge(s["x_loaded"], 16 * (c + 1))
                layer_norm(nc, dve, s["ln0_steps"], c, xn_tok, xn_tok, ln_tmp,
                           s["passed_dve"])
                dve.wait_ge(s["xn_turned"], c + 1)
                for k in range(KD):
                    last = v.tensor_scalar(xnT[:, k, :], ps[:, k, :], col("ln_g", k), col("ln_b", k),
                                           ALU.mult, ALU.add)
                last.then_inc(s["xnT_ready"], 1)
                v.tensor_copy(x_br[:, :, 0:TAPS - 1], halo[:]).then_inc(s["halo_put"], 1)
                dve.wait_ge(s["halo_put"], c + 1)
                for tap in range(TAPS):
                    for e in range(DB):
                        w = col("conv_w", tap * DB + e)
                        src = x_br[:, e, tap:tap + CH]
                        if tap == 0:
                            dve.wait_ge(s["xbr_copied"], c * DB + e + 1)
                            one = v.tensor_scalar(conv[:, e, :], src, w, col("conv_b", e),
                                                  ALU.mult, ALU.add)
                        else:
                            dve.wait_ge(s["conv_steps"], c * DB * TAPS + (tap - 1) * DB + e + 1)
                            one = v.scalar_tensor_tensor(conv[:, e, :], src, w, conv[:, e, :],
                                                         ALU.mult, ALU.add)
                        one.then_inc(s["conv_steps"], 1)
                keep = cols[:, bass.ds(COL_AT["keep"] + c + 1, 1)]
                dve.wait_ge(s["conv_steps"], (c + 1) * DB * TAPS)
                v.tensor_scalar(halo[:], x_br[:, :, CH:], keep, None, ALU.mult)\
                    .then_inc(s["halo_kept"], 1)
                dve.wait_ge(s["bc_mm"], c + 1)
                src = ps[0:6 * NS, 4, :]
                steps = s["bc_steps"]
                v.tensor_copy(bc3[:], src).then_inc(steps, 1)
                dve.wait_ge(steps, c * 5 + 1)
                v.tensor_tensor(bc_rest, src, bc3[:], ALU.subtract).then_inc(steps, 1)
                dve.wait_ge(steps, c * 5 + 2)
                v.tensor_copy(bc_mid, bc_rest).then_inc(steps, 1)
                dve.wait_ge(steps, c * 5 + 3)
                v.tensor_copy(bc3[2 * NS:4 * NS, :], bc_mid[2 * NS:4 * NS, :]).then_inc(steps, 1)
                v.tensor_tensor(bc3[4 * NS:, :], bc_rest[4 * NS:, :], bc_mid[4 * NS:, :],
                                ALU.subtract).then_inc(steps, 1)
                dve.wait_ge(s["halo_kept"], c + 1)
                for m in range(DB):
                    dve.wait_ge(s["delta_mm"], c * DB + m + 1)
                    v.tensor_scalar(pre[:, m, :], ps[:, m, :], col("b_delta", m), None, ALU.add)\
                        .then_inc(s["pre_ready"], 1)
                for i in range(2):
                    half = slice(2 * i, 2 * i + 2)
                    dve.wait_ge(s["soft_ready"], c * 6 + 3 * i + 3)
                    v.scalar_tensor_tensor(delta[:, half], pre[:, half], 0.0, soft[:, half],
                                           ALU.max, ALU.add).then_inc(s["delta_ready"], 1)
                    dve.wait_ge(s["delta_ready"], c * 2 + i + 1)
                    v.tensor_tensor(du[:, half], delta[:, half], xb[:, half], ALU.mult)\
                        .then_inc(s["du_ready"], 1)

            def b_times(c, n):
                if n == 0:
                    dve.wait_ge(s["du_ready"], (c + 1) * 2)
                dve.wait_ge(s["b_mm"], c * NS + n + 1)
                at_least(dve, s["h_ready"], (c * NS + n) * DB)
                v.tensor_tensor(bx[:], du[:], ps[:, 4:5, :].to_broadcast([P, DB, CH]), ALU.mult)\
                    .then_inc(s["bx_ready"], 1)

            def scans(c, n):
                for m in range(DB):
                    if n >= 2:
                        dve.wait_ge(s["y_mm"], (c * NS + n - 2) * DB + m + 1)
                    dve.wait_ge(s["decay_ready"], (c * NS + n) * DB + m + 1)
                    if m == 0:
                        dve.wait_ge(s["bx_ready"], c * NS + n + 1)
                    v.tensor_tensor_scan(h[:, n % 2, m, :], decay[:, m, :], bx[:, m, :],
                                         state[:, n, m:m + 1], ALU.mult, ALU.add)\
                        .then_inc(s["h_ready"], 1)

            def keep_state(c, n):
                keep = cols[:, bass.ds(COL_AT["keep"] + c + 1, 1)]
                dve.wait_ge(s["h_ready"], (c * NS + n + 1) * DB)
                v.tensor_scalar(state[:, n, :], h[:, n % 2, :, CH - 1], keep, None, ALU.mult)\
                    .then_inc(s["state_kept"], 1)

            def gated(c):
                dve.wait_ge(s["y_mm"], (c + 1) * NS * DB)
                v.tensor_tensor(g[:], ps[:, 0:DB, :], gate[:], ALU.mult).then_inc(s["g_ready"], 1)

            def norm1(c):
                dve.wait_ge(s["out_mm"], c + 1)
                dve.wait_ge(s["residual_loaded"], 16 * (c + 1))
                v.scalar_tensor_tensor(x1_tok[:], x1_tok[:], 2.0,
                                       ps[:, 4:6, :].rearrange("p a (s n) -> p (a s) n", n=D),
                                       ALU.mult, ALU.add).then_inc(s["r_ready"], 1)
                dve.wait_ge(s["r_ready"], c + 1)
                layer_norm(nc, dve, s["ln1_steps"], c, x1_tok[:], x1_tok[:], ln_tmp,
                           s["passed_dve"])

            def weigh(c):
                steps = s["router_steps"]
                wait_full(dve, c, ("logits", 0))
                read(v.tensor_tensor(lg[:], bank(("logits", 0))[:, 0:TT * NE].rearrange("p (s e) -> p s e", e=NE),
                                     r_b2[:].unsqueeze(1).to_broadcast([P, TT, NE]), ALU.add), ("logits", 0))
                wait_read(dve, c, ("logits", 0))
                v.tensor_reduce(lmax[:], lg[:], AX.X, ALU.max).then_inc(steps, 1)
                dve.wait_ge(steps, c * 8 + 1)
                v.tensor_tensor(lg[:], lg[:], lmax[:].unsqueeze(2).to_broadcast([P, TT, NE]),
                                ALU.subtract).then_inc(steps, 1)
                dve.wait_ge(s["lexp_ready"], c + 1)
                v.tensor_reduce(lmax[:], lexp[:], AX.X, ALU.add).then_inc(steps, 1)
                dve.wait_ge(steps, c * 8 + 3)
                v.reciprocal(lmax[:], lmax[:]).then_inc(steps, 1)
                dve.wait_ge(steps, c * 8 + 4)
                v.tensor_tensor(prob[:], lexp[:], lmax[:].unsqueeze(2).to_broadcast([P, TT, NE]),
                                ALU.mult).then_inc(steps, 1)
                dve.wait_ge(steps, c * 8 + 5)
                for j in range(NE):
                    for lo, hi, op in ((0, j, ALU.is_gt), (j + 1, NE, ALU.is_ge)):
                        if hi > lo:
                            last = v.tensor_tensor(beats[:, j, :, lo:hi],
                                                   prob[:, :, j:j + 1].to_broadcast([P, TT, hi - lo]),
                                                   prob[:, :, lo:hi], op)
                last.then_inc(steps, 1)
                dve.wait_ge(steps, c * 8 + 6)
                v.tensor_reduce(rank[:], beats[:].rearrange("p j s e -> p s e j"), AX.X, ALU.add)\
                    .then_inc(steps, 1)
                dve.wait_ge(steps, c * 8 + 7)
                v.scalar_tensor_tensor(cw[:], rank[:], 2.0, prob[:], ALU.is_lt, ALU.mult)\
                    .then_inc(steps, 1)

            def base(c):
                for j in range(2):
                    wait_full(dve, c, ("cwT", j))
                    read(v.tensor_copy(cwT[:, 2 * j:2 * j + 2, :].rearrange("e s p -> e (s p)"),
                                       bank(("cwT", j))[0:NE, 0:2 * P]), ("cwT", j))
                dve.wait_ge(s["x1T_ready"], c + 1)
                for j in range(2):
                    wait_full(dve, c, ("base", j))
                    rows = x1_tok[:, 2 * j:2 * j + 2, :].rearrange("p s n -> p (s n)")
                    read(v.tensor_tensor(rows, bank(("base", j)), rows, ALU.add), ("base", j))

            def down(c, e, pair):
                key = ("down", e, pair)
                wait_full(dve, c, key)
                wait_read(dve, c, ("down", e - 1, pair) if e else ("base", pair))
                for i in range(2):
                    t = 2 * pair + i
                    last = v.scalar_tensor_tensor(x1_tok[:, t, :], bank(key)[:, i * D:(i + 1) * D],
                                                  cw[:, t, e:e + 1], x1_tok[:, t, :],
                                                  ALU.mult, ALU.add)
                read(last, key)

            def experts(c, n):
                if n == 0:
                    weigh(c)
                for j in quarters(n):
                    if j == 2:
                        base(c)
                    if j % 4 >= 2:
                        down(c, j // 4, j % 4 - 2)

            def norm2(c):
                for pair in range(2):
                    wait_read(dve, c, ("down", NE - 1, pair))
                layer_norm(nc, dve, s["ln2_steps"], c, x1_tok[:], x1_tok[:], ln_tmp,
                           s["passed_dve"])

            def keys(c):
                wait_full(dve, c, ("cross", 1))
                wait_read(dve, c, ("cross", 0))
                read(v.scalar_tensor_tensor(cr[:, 0, :], bank(("cross", 1))[0:CX], xcols[:, 1:2],
                                            cr[:, 0, :], ALU.add, ALU.mult), ("cross", 1))
                wait_full(dve, c, ("cross", 3))
                wait_read(dve, c, ("cross", 2))
                read(v.scalar_tensor_tensor(cr[:, 1, :], bank(("cross", 3))[0:CX], xcols[:, 3:4],
                                            cr[:, 1, :], ALU.add, ALU.mult), ("cross", 3))
                wait_read(dve, c, ("cross", 3))
                wait_read(dve, c, ("cross", 1))
                v.tensor_tensor(cr[:, 0, :], cr[:, 0, :], cr[:, 1, :], ALU.subtract)\
                    .then_inc(s["crossed"], 1)
                for m in range(KD):
                    wait_full(dve, c, ("kadd", m))
                    read(v.tensor_tensor(kt[:, m, :], bank(("kadd", m)), qk[:, 2 + m, :], ALU.add),
                         ("kadd", m))
                    wait_read(dve, c, ("kadd", m))
                    v.tensor_scalar(kt[:, m, :], kt[:, m, :], temp[:, 0:1], None, ALU.mult)\
                        .then_inc(s["k_steps"], 2)
                wait_read(dve, c, ("kb", 0))
                steps = s["kb_steps"]
                at_least(dve, s["kb_stored"], 16 * c)
                split3(dve, v, kb_f, kb_f, [kb_parts[:, i, :] for i in range(3)], steps, c * 5)

            def split3(eng, e, src, rest, part, steps, base):
                e.tensor_copy(part[0], src).then_inc(steps, 1)
                eng.wait_ge(steps, base + 1)
                e.tensor_tensor(rest, src, part[0], ALU.subtract).then_inc(steps, 1)
                eng.wait_ge(steps, base + 2)
                e.tensor_copy(part[1], rest).then_inc(steps, 1)
                eng.wait_ge(steps, base + 3)
                e.tensor_tensor(part[2], rest, part[1], ALU.subtract).then_inc(steps, 2)

            v.memset(halo[:], 0.0).then_inc(s["setup_dve"], 1)
            v.memset(state[:], 0.0).then_inc(s["setup_dve"], 1)
            v.memset(beats[:], 0.0).then_inc(s["setup_dve"], 1)
            dve.wait_ge(s["w_mamba"], W_MAMBA)
            v.tensor_copy(sel[:], part_rows[:])\
                .then_inc(s["setup_dve"], 1)
            for m in range(DB):
                last = v.tensor_scalar(diag_d[:, m, :], ident[:], col("d_skip", m), None, ALU.mult)
            last.then_inc(s["setup_dve"], 1)
            dve.wait_ge(s["neg_ready"], 1)
            v.tensor_scalar(neg_a[:], neg_a[:], -1.0, None, ALU.mult).then_inc(s["setup_dve"], 1)
            dve.wait_ge(s["setup_dve"], 6)

            def chunk(c, before):
                front(c)
                b_times(c, 0)
                for n in range(NS):
                    scans(c, n)
                    keep_state(c, n)
                    if n + 1 < NS:
                        b_times(c, n + 1)
                    if before is not None and n > 0:
                        experts(before, n - 1)
                gated(c)
                if before is not None:
                    experts(before, NS - 1)
                    norm2(before)
                norm1(c)
                if before is not None:
                    keys(before)

            chunk(0, None)
            dve.wait_ge(s["w_moe"], W_MOE)
            with dve.Fori(1, chunks) as c:
                chunk(c, c - 1)
            for n in range(NS):
                experts(chunks - 1, n)
            norm2(chunks - 1)
            keys(chunks - 1)

        @block.gpsimd
        def _(pool):
            def times_c(c, n):
                pool.wait_ge(s["c_copied"], c * NS + n + 1)
                pool.wait_ge(s["h_ready"], (c * NS + n + 1) * DB)
                pool.wait_ge(s["state_kept"], c * NS + n + 1)
                nc.gpsimd.tensor_tensor(h[:, n % 2], h[:, n % 2], c_sb[:, n % 2:n % 2 + 1, :].to_broadcast([P, DB, CH]),
                                        ALU.mult).then_inc(s["hc_ready"], 1)

            def split(c, i, src, semaphore, value):
                steps, base = s["parts_steps"], c * 8 + 4 * i
                part = [parts[:, j] for j in range(3)]
                left = src
                wait_alone(pool, s["passed_pool"], semaphore, value)
                nc.gpsimd.tensor_copy(part[0], src).then_inc(steps, 1)
                pool.wait_ge(steps, base + 1)
                nc.gpsimd.tensor_tensor(left, src, part[0], ALU.subtract).then_inc(steps, 1)
                wait_alone(pool, s["passed_pool"], steps, base + 2)
                nc.gpsimd.tensor_copy(part[1], left).then_inc(steps, 1)
                pool.wait_ge(steps, base + 3)
                nc.gpsimd.tensor_tensor(part[2], left, part[1], ALU.subtract).then_inc(steps, 1)

            def qkv(c):
                wait_read(pool, c, ("q", 0))
                wait_read(pool, c, ("q", 1))
                split(c, 0, qk[:, 0:2, :], s["k_stored"], 32 * c)
                pool.wait_ge(s["k_steps"], 4 * c + 4)
                split(c, 1, kt, s["q_stored"], 32 * c + 32)

            pool.wait_ge(s["setup_dve"], 6)
            for n in range(NS):
                times_c(0, n)
            with pool.Fori(1, chunks) as c:
                for n in range(NS):
                    times_c(c, n)
                qkv(c - 1)
            qkv(chunks - 1)


HEADS = B * NH
QC = L // CH
KT = L // P
SLOTS = QC * KT // 2
ROT = 4
STACK = 6 * HD
K_MAX = STACK + 3
K_ALL = K_MAX + 2
VW = 2 * HD
Q_PARTS = (0, 0, 1, 0, 2, 1)
K_PARTS = (0, 1, 0, 2, 0, 1)
MAX_USES = 4 * KT + 1


def attention_ffn(nc, a, scr, out, heads=HEADS, chunks=NCH):
    batches, quads = heads // NH, NH // ROT
    with ExitStack() as ctx:
        def sb(name, shape, dt=F32):
            return ctx.enter_context(nc.sbuf_tensor(name, shape, dt))

        def sem(name):
            return ctx.enter_context(nc.semaphore(name))

        ident = sb("ident2", [P, P])
        fold = sb("fold", [P, VW])
        wo = sb("wo", [P, KD, D])
        w1 = sb("w1", [P, KD, HB * P])
        w2 = sb("w2", [P, HB, D])
        b1 = sb("b1", [P, HB])
        bo = sb("bo", [P, D])
        b2 = sb("b2", [P, D])
        v_all = sb("v_all", [P, B * KT, D])
        o_all = sb("o_all", [P, B * KT, D])
        qs = sb("qs", [P, ROT, L], BF16)
        ks = sb("ks", [P, ROT, L], BF16)
        vh = sb("vh", [P, ROT, KT, VW])
        probs = sb("probs", [P, 4, 2 * CH])
        av = sb("av", [P, 2, CH])
        inv = sb("inv", [P, 2, TT])
        tile_max = sb("tile_max", [P, 2, KT, 4])
        row_max = sb("row_max", [P, KT])
        neg = sb("neg", [KT, P])
        neg_parts = sb("neg_parts", [KT, 2, P], BF16)
        xr = sb("xr", [P, 2, TT, D])
        o_tok = sb("o_tok", [P, TT, D])
        oT = sb("oT", [P, KD, CH])
        x3 = sb("x3", [P, TT, D])
        x3b = sb("x3b", [P, TT, D])
        x3T = sb("x3T", [P, KD, CH])
        hid = sb("hid_f", [P, HB, CH])
        ysum = sb("ysum", [P, TT, D])
        y = sb("y", [P, TT, D])
        ln_tmp = ln_buffers(sb, "lnf")
        ps = ctx.enter_context(nc.psum_tensor("ps2", [P, 8, CH], F32))

        names = """loads v_loaded weights setup max_mm max_read max_ready neg_steps neg_stored
            v_staged scores_mm probs_ready av_mm av_copied fold_mm inv_ready o_written
            bias_added o_staged o_turned oT_ready wo_mm r_ready ln3_steps x3_turned x3T_ready
            x3b_ready up_mm hid_ready down_mm sum_ready ln4_steps y_stored
            passed_sp passed_dve passed_pool""".split()
        s = {n: sem(n) for n in names}
        stack_loaded = [sem(f"stack_loaded{j}") for j in range(ROT)]
        neg_loaded = [sem(f"neg_loaded{j}") for j in range(ROT)]
        x2_loaded = [sem(f"x2_loaded{j}") for j in range(2)]
        STACK_DMAS = 16 * (2 * 6 + 1)

        block = ctx.enter_context(nc.Block())

        @block.sync
        def _(sp):
            def load_stack(u, j, slots):
                wait_alone(sp, s["passed_sp"], s["scores_mm"], slots)
                head = u & (HEADS - 1)
                rows = bass.ds(head * HD, HD)
                for i in range(6):
                    for dst, name, part in ((qs, "q", Q_PARTS[i]), (ks, "k", K_PARTS[i])):
                        sp.dma_start(dst[i * HD:(i + 1) * HD, j, :].rearrange("p (j t) -> p j t", t=CH),
                                     scr[name][rows, :, part, :]).then_inc(stack_loaded[j], 16)
                sp.dma_start(ks[STACK:K_MAX, j, :].rearrange("p (j t) -> p j t", t=CH),
                             scr["kb"][bass.ds(head, 1), :, :, :].rearrange("o j p t -> p (o j) t"))\
                    .then_inc(stack_loaded[j], 16)

            def load_neg(u, j):
                sp.wait_ge(s["neg_steps"], 3 * u + 3)
                sp.dma_start(scr["neg"][j].rearrange("i (q p) -> q i p", p=P), neg_parts[:])\
                    .then_inc(s["neg_stored"], 16)
                wait_alone(sp, s["passed_sp"], s["neg_stored"], 16 * (u + 1))
                sp.dma_start(qs[K_MAX:K_ALL, j, :], scr["neg"][j]).then_inc(neg_loaded[j], 16)

            sp.wait_ge(s["setup"], 4)
            for t, name in ((ident, "ident"), (fold, "fold")):
                sp.dma_start(t[:], a[name]).then_inc(s["loads"], 16)
            for u in range(3):
                load_stack(u, u, 0)
            for b in range(B):
                sp.dma_start(v_all[:, b * KT:(b + 1) * KT, :],
                             scr["v"][b * L:(b + 1) * L, :].rearrange("(t p) n -> p t n", p=P))\
                    .then_inc(s["v_loaded"], 16)
            for t, name in ((wo, "wo"), (w1, "w1"), (w2, "w2"), (b1, "b1")):
                sp.dma_start(t[:], a[name]).then_inc(s["weights"], 16)
            for t, name in ((bo, "bo"), (b2, "b2")):
                sp.dma_start(t[:], a[name].partition_broadcast(P)).then_inc(s["weights"], 16)
            load_neg(0, 0)
            with sp.Fori(0, heads // ROT) as r:
                for j in range(ROT):
                    u = r * ROT + j
                    load_neg(u + 1, (j + 1) % ROT)
                    load_stack(u + 3, (j + 3) % ROT, u * SLOTS)

            def load_x2(c, j):
                sp.dma_start(xr[:, j], scr["x2"][bass.ds(c * CH, CH), :].rearrange("(s p) n -> p s n", p=P))\
                    .then_inc(x2_loaded[j], 16)

            def store_y(c):
                sp.wait_ge(s["ln4_steps"], (c + 1) * LN_STEPS)
                sp.dma_start(out[bass.ds(c * CH, CH), :].rearrange("(s p) n -> p s n", p=P), y[:])\
                    .then_inc(s["y_stored"], 16)

            load_x2(0, 0)
            load_x2(1, 1)
            with sp.Fori(0, chunks // 2) as r:
                for j in range(2):
                    c = 2 * r + j
                    wait_alone(sp, s["passed_sp"], s["bias_added"], c + 1)
                    load_x2((c + 2) & (NCH - 1), j)
                    store_y(c)
            sp.wait_ge(s["y_stored"], 16 * chunks)
            for j in range(2):
                sp.wait_ge(x2_loaded[j], 16 * (chunks // 2 + 1))
            for j in range(ROT):
                sp.wait_ge(stack_loaded[j], (heads // ROT + (j < 3)) * STACK_DMAS)
            sp.wait_ge(neg_loaded[0], 16 * (heads // ROT + 1))
            sp.wait_ge(s["neg_stored"], 16 * (heads + 1))

        @block.tensor
        def _(pe):
            mm = nc.tensor.matmul

            def one_max(u, turn, j, i):
                if i == 0:
                    pe.wait_ge(stack_loaded[j], (turn + 1) * STACK_DMAS)
                    at_least(pe, s["max_read"], u * MAX_USES)
                else:
                    at_least(pe, s["max_read"], u * MAX_USES + i - 1)
                t, k = i // 4, i % 4
                mm(ps[:, 6 + i % 2, :], qs[0:K_MAX, j, t * P:(t + 1) * P],
                   ks[0:K_MAX, j, k * CH:(k + 1) * CH], start=True, stop=True)\
                    .then_inc(s["max_mm"], 1)

            def turn_max(u):
                pe.wait_ge(s["max_ready"], u + 1)
                pe.wait_ge(s["max_read"], u * MAX_USES + MAX_USES - 1)
                nc.tensor.transpose(ps[0:KT, 6, 0:P], row_max[:], ident[:]).then_inc(s["max_mm"], 1)

            def scores(u, turn, j, slot):
                if slot == 0:
                    pe.wait_ge(neg_loaded[j], 16 * (turn + 1))
                at_least(pe, s["probs_ready"], u * SLOTS + slot - 1 if slot else u * SLOTS)
                qc, kp = slot // (KT // 2), slot % (KT // 2)
                for i in range(2):
                    k = 2 * kp + i
                    last = mm(ps[:, 2 * (slot % 2) + i, :], ks[0:K_ALL, j, k * P:(k + 1) * P],
                              qs[0:K_ALL, j, qc * CH:(qc + 1) * CH], start=True, stop=True)
                last.then_inc(s["scores_mm"], 1)

            def values(u, j, group):
                qc, quad = group // (KT // 4), group % (KT // 4)
                pe.wait_ge(s["probs_ready"], u * SLOTS + 2 * group + 2)
                if group == 0:
                    pe.wait_ge(s["v_staged"], u + 1)
                if quad == 0:
                    at_least(pe, s["o_written"], u * QC + qc - 1 if qc else u * QC)
                for i in range(4):
                    k = 4 * quad + i
                    last = mm(ps[i * VW:(i + 1) * VW, 4 + qc % 2, :], vh[:, j, k, :],
                              probs[:, (2 * group + i // 2) % 4, (i % 2) * CH:(i % 2 + 1) * CH],
                              start=quad == 0, stop=quad == KT // 4 - 1)
                last.then_inc(s["av_mm"], 1)

            def fold_groups(u, qc):
                pe.wait_ge(s["av_copied"], u * QC + qc + 1)
                for i in range(TT):
                    last = mm(ps[:, 4 + qc % 2, i * VW:(i + 1) * VW],
                              av[:, qc % 2, i * P:(i + 1) * P], fold[:], start=True, stop=True)
                last.then_inc(s["fold_mm"], 1)

            def head(u, r, j):
                last_group = QC * KT // 4 - 1
                for slot in range(SLOTS):
                    scores(u, r, j, slot)
                    for i in (2 * slot, 2 * slot + 1):
                        if slot < SLOTS // 2:
                            one_max(u + 1, r + (j + 1) // ROT, (j + 1) % ROT, 2 * KT + i)
                        else:
                            if i == SLOTS:
                                turn_max(u + 1)
                            one_max(u + 2, r + (j + 2) // ROT, (j + 2) % ROT, i - SLOTS)
                    if slot % 2 and slot > 2:
                        group = (slot - 3) // 2
                        values(u, j, group)
                        if group >= 5 and group % 4 == 1:
                            fold_groups(u, group // 4 - 1)
                values(u, j, last_group)
                fold_groups(u, QC - 1)

            pe.wait_ge(s["loads"], 32)
            for i in range(4 * KT):
                one_max(0, 0, 0, i)
            turn_max(0)
            for i in range(2 * KT):
                one_max(1, 0, 1, i)
            with pe.Fori(0, heads // ROT) as r:
                for j in range(ROT):
                    head(r * ROT + j, r, j)

            def output_projection(c):
                pe.wait_ge(s["o_staged"], c + 1)
                for k in range(KD):
                    for i in range(TT):
                        last = nc.tensor.transpose(ps[:, 4 + k, i * P:(i + 1) * P],
                                                   o_tok[:, i, k * P:(k + 1) * P], ident[:])
                last.then_inc(s["o_turned"], 1)
                pe.wait_ge(s["oT_ready"], c + 1)
                for i in range(TT):
                    for k in range(KD):
                        last = mm(ps[:, 4 + i // 2, (i % 2) * D:(i % 2 + 1) * D],
                                  oT[:, k, i * P:(i + 1) * P], wo[:, k, :],
                                  start=k == 0, stop=k == KD - 1)
                last.then_inc(s["wo_mm"], 1)
                pe.wait_ge(s["ln3_steps"], (c + 1) * LN_STEPS)
                for k in range(KD):
                    for i in range(TT):
                        last = nc.tensor.transpose(ps[:, 4 + k, i * P:(i + 1) * P],
                                                   x3[:, i, k * P:(k + 1) * P], ident[:])
                last.then_inc(s["x3_turned"], 1)

            def feed_forward(c):
                pe.wait_ge(s["x3T_ready"], c + 1)
                for i in range(HB):
                    at_least(pe, s["hid_ready"], c * HB + i - 3 if i > 3 else c * HB)
                    for k in range(KD):
                        last = mm(ps[:, i % 4, :], w1[:, k, i * P:(i + 1) * P], x3T[:, k, :],
                                  start=k == 0, stop=k == KD - 1)
                    last.then_inc(s["up_mm"], 1)
                pe.wait_ge(s["hid_ready"], (c + 1) * HB)
                at_least(pe, s["sum_ready"], c)
                for i in range(TT):
                    for k in range(HB):
                        last = mm(ps[:, 6 + i // 2, (i % 2) * D:(i % 2 + 1) * D],
                                  hid[:, k, i * P:(i + 1) * P], w2[:, k, :],
                                  start=k == 0, stop=k == HB - 1)
                last.then_inc(s["down_mm"], 1)

            pe.wait_ge(s["weights"], 96)
            pe.wait_ge(s["o_written"], heads * QC)
            pe.wait_ge(s["max_read"], (heads + 1) * MAX_USES + 2 * KT)
            with pe.Fori(0, chunks) as c:
                output_projection(c)
                feed_forward(c)

        @block.scalar
        def _(act):
            fn = nc.scalar.activation

            def head(u, j):
                for slot in range(SLOTS):
                    act.wait_ge(s["scores_mm"], u * SLOTS + slot + 1)
                    at_least(act, s["av_mm"], u * (SLOTS // 2) + (slot - 4) // 2 + 1
                             if slot >= 4 else u * (SLOTS // 2))
                    b = 2 * (slot % 2)
                    fn(probs[:, slot % 4, :], ps[:, b:b + 2, :].rearrange("p a n -> p (a n)"), ACT.Exp)\
                        .then_inc(s["probs_ready"], 1)
                    if slot % 8 == 4 and slot > 8:
                        copy_values(u, slot // 8 - 1)
                copy_values(u, QC - 1)

            def copy_values(u, qc):
                act.wait_ge(s["av_mm"], u * (SLOTS // 2) + (qc + 1) * (KT // 4))
                at_least(act, s["fold_mm"], u * QC + qc - 1 if qc else u * QC)
                fn(av[:, qc % 2, :], ps[:, 4 + qc % 2, :], ACT.Copy).then_inc(s["av_copied"], 1)

            with act.Fori(0, heads // ROT) as r:
                for j in range(ROT):
                    head(r * ROT + j, j)

            act.wait_ge(s["weights"], 96)
            with act.Fori(0, chunks) as c:
                act.wait_ge(s["o_turned"], c + 1)
                fn(oT[:], ps[:, 4:6, :], ACT.Copy).then_inc(s["oT_ready"], 1)
                act.wait_ge(s["x3_turned"], c + 1)
                fn(x3T[:], ps[:, 4:6, :], ACT.Copy).then_inc(s["x3T_ready"], 1)
                at_least(act, s["down_mm"], c)
                for i in range(HB):
                    act.wait_ge(s["up_mm"], c * HB + i + 1)
                    fn(hid[:, i, :], ps[:, i % 4, :], ACT.Relu, bias=b1[:, i:i + 1])\
                        .then_inc(s["hid_ready"], 1)

        @block.vector
        def _(dve):
            v = nc.vector

            def one_max(u, i):
                dve.wait_ge(s["max_mm"], u * MAX_USES + i + 1)
                if i == 0:
                    at_least(dve, s["max_ready"], u - 1)
                v.tensor_reduce(tile_max[:, 0, i // 4, i % 4:i % 4 + 1], ps[:, 6 + i % 2, :],
                                AX.X, ALU.max).then_inc(s["max_read"], 1)

            def row_maxima(u):
                dve.wait_ge(s["max_read"], u * MAX_USES + MAX_USES - 1)
                v.tensor_reduce(row_max[:], tile_max[:, 0], AX.X, ALU.max).then_inc(s["max_ready"], 1)

            def negate(u):
                dve.wait_ge(s["max_mm"], u * MAX_USES + MAX_USES)
                at_least(dve, s["neg_steps"], 3 * u)
                v.tensor_scalar(neg[:], ps[0:KT, 6, 0:P], -1.0, None, ALU.mult)\
                    .then_inc(s["max_read"], 1)
                dve.wait_ge(s["max_read"], (u + 1) * MAX_USES)
                at_least(dve, s["neg_stored"], 16 * u)
                v.tensor_copy(neg_parts[:, 0, :], neg[:]).then_inc(s["neg_steps"], 1)
                dve.wait_ge(s["neg_steps"], 3 * u + 1)
                v.tensor_tensor(neg_parts[:, 1, :], neg[:], neg_parts[:, 0, :], ALU.subtract)\
                    .then_inc(s["neg_steps"], 2)

            def normalise(u, h0, qc):
                dve.wait_ge(s["fold_mm"], u * QC + qc + 1)
                o = ps[:, 4 + qc % 2, 0:TT * VW].rearrange("p (t n) -> p t n", n=VW)
                v.reciprocal(inv[:, qc % 2, :], o[:, :, HD]).then_inc(s["inv_ready"], 1)
                dve.wait_ge(s["inv_ready"], u * QC + qc + 1)
                b, hd = h0
                v.tensor_tensor(o_all[:, bass.ds(b * KT + qc * TT, TT), bass.ds(hd * HD, HD)],
                                o[:, :, 0:HD],
                                inv[:, qc % 2, :].unsqueeze(2).to_broadcast([P, TT, HD]), ALU.mult)\
                    .then_inc(s["o_written"], 1)

            def head(u, h0):
                for slot in range(SLOTS):
                    for i in (2 * slot, 2 * slot + 1):
                        if slot < SLOTS // 2:
                            one_max(u + 1, 2 * KT + i)
                            if i == 2 * KT - 1:
                                row_maxima(u + 1)
                        else:
                            if i == SLOTS:
                                negate(u + 1)
                            one_max(u + 2, i - SLOTS)
                    if slot % 8 == 5 and slot > 8:
                        normalise(u, h0, slot // 8 - 1)
                normalise(u, h0, QC - 1)

            v.memset(qs[STACK:, :, :], 1.0).then_inc(s["setup"], 1)
            v.memset(ks[STACK:, :, :], 1.0).then_inc(s["setup"], 1)
            v.memset(vh[:, :, :, HD:], 0.0).then_inc(s["setup"], 1)
            dve.wait_ge(s["setup"], 3)
            v.memset(vh[:, :, :, HD:HD + 1], 1.0).then_inc(s["setup"], 1)
            for i in range(4 * KT):
                one_max(0, i)
            row_maxima(0)
            negate(0)
            for i in range(2 * KT):
                one_max(1, i)
            with dve.Fori(0, batches) as b:
                with dve.Fori(0, quads) as quad:
                    for j in range(ROT):
                        hd = quad * ROT + j
                        head(b * NH + hd, (b, hd))

            with dve.Fori(0, chunks) as c:
                at_least(dve, s["o_turned"], c)
                v.tensor_copy(o_tok[:], o_all[:, bass.ds(c * TT, TT), :]).then_inc(s["o_staged"], 1)
                dve.wait_ge(s["wo_mm"], c + 1)
                dve.wait_ge(s["bias_added"], c + 1)
                at_least(dve, s["x3b_ready"], c)
                v.tensor_tensor(x3[:], ps[:, 4:6, :].rearrange("p a (s n) -> p (a s) n", n=D),
                                x3b[:], ALU.add).then_inc(s["r_ready"], 1)
                dve.wait_ge(s["r_ready"], c + 1)
                layer_norm(nc, dve, s["ln3_steps"], c, x3[:], x3[:], ln_tmp,
                           s["passed_dve"])
                dve.wait_ge(s["down_mm"], c + 1)
                dve.wait_ge(s["x3b_ready"], c + 1)
                v.tensor_tensor(ysum[:], ps[:, 6:8, :].rearrange("p a (s n) -> p (a s) n", n=D),
                                y[:], ALU.add).then_inc(s["sum_ready"], 1)
                dve.wait_ge(s["sum_ready"], c + 1)
                layer_norm(nc, dve, s["ln4_steps"], c, ysum[:], y[:], ln_tmp,
                           s["passed_dve"])

        @block.gpsimd
        def _(pool):
            def stage(u, b, hd, j):
                free = (u - ROT + 1) * (SLOTS // 2)
                wait_alone(pool, s["passed_pool"], s["av_mm"], free)
                column = bass.ds(hd * HD, HD)
                nc.gpsimd.tensor_copy(vh[:, j, :, 0:HD],
                                      v_all[:, bass.ds(b * KT, KT), bass.ds(hd * HD, HD)])\
                    .then_inc(s["v_staged"], 1)

            pool.wait_ge(s["setup"], 4)
            pool.wait_ge(s["v_loaded"], 32)
            for j in range(ROT):
                stage(j, 0, j, j)
            with pool.Fori(1, quads) as quad:
                for j in range(ROT):
                    stage(quad * ROT + j, 0, quad * ROT + j, j)
            with pool.Fori(1, batches) as b:
                with pool.Fori(0, quads) as quad:
                    for j in range(ROT):
                        hd = quad * ROT + j
                        stage(b * NH + hd, b, hd, j)

            pool.wait_ge(s["weights"], 96)
            with pool.Fori(0, chunks // 2) as r:
                for j in range(2):
                    c = 2 * r + j
                    pool.wait_ge(x2_loaded[j], 16 * (r + 1))
                    nc.gpsimd.tensor_tensor(x3b[:], xr[:, j], bo[:].unsqueeze(1).to_broadcast([P, TT, D]),
                                            ALU.add).then_inc(s["bias_added"], 1)
                    pool.wait_ge(s["ln3_steps"], (c + 1) * LN_STEPS)
                    at_least(pool, s["y_stored"], 16 * c)
                    nc.gpsimd.tensor_tensor(y[:], x3[:], b2[:].unsqueeze(1).to_broadcast([P, TT, D]),
                                            ALU.add).then_inc(s["x3b_ready"], 1)


COL_ORDER = [("ln_g", KD), ("ln_b", KD), ("conv_w", TAPS * DB), ("conv_b", DB), ("b_delta", DB),
             ("d_skip", DB), ("r_b1", RB), ("e_b1", NE * HB), ("bq", KD), ("bk", KD), ("bv", KD),
             ("keep", NCH + 1)]
COL_AT, _n = {}, 0
for _name, _width in COL_ORDER:
    COL_AT[_name] = _n
    _n += _width
N_COLS = _n


def lay_out(i):
    def blocks(w):
        return np.ascontiguousarray(w.reshape(-1, P, w.shape[1]).transpose(1, 0, 2))

    def column(b):
        return b.reshape(-1, P).T

    a = {"x": i["L0_attn_x"].reshape(TOK, D)}
    a["ident"] = np.eye(P, dtype=np.float32)
    a["part_rows"] = np.tile(np.eye(2 * NS, dtype=np.float32), (3, 1))
    keep = np.ones((P, NCH + 1), np.float32)
    keep[:, ::NCH // B] = 0.0
    conv_w = i["L0_attn_conv_w"][:, 0, :]
    cols = {"ln_g": column(i["L0_attn_ln_g"]), "ln_b": column(i["L0_attn_ln_b"]),
            "conv_w": conv_w.reshape(DB, P, TAPS).transpose(1, 2, 0).reshape(P, -1),
            "conv_b": column(i["L0_attn_conv_b"]), "b_delta": column(i["L0_attn_b_delta"]),
            "d_skip": column(i["L0_attn_Dp"]), "r_b1": column(i["L0_ffn_rb1"]),
            "e_b1": column(i["L0_ffn_be1"].reshape(-1)), "bq": column(i["L1_attn_bq"]),
            "bk": column(i["L1_attn_bk"]), "bv": column(i["L1_attn_bv"]), "keep": keep}
    a["cols"] = np.concatenate([cols[n] for n, _ in COL_ORDER], axis=1)
    a["log_a"] = i["L0_attn_log_A"].reshape(DB, P, NS).transpose(1, 2, 0).reshape(P, -1)
    a["w_in"], a["w_delta"] = blocks(i["L0_attn_W_in"]), blocks(i["L0_attn_W_delta"])
    bc = np.concatenate([i["L0_attn_W_b"], i["L0_attn_W_c"]] * 3, axis=1)
    a["w_bc3"], a["w_out"] = blocks(bc), blocks(i["L0_attn_W_out"])
    a["r_w1"], a["r_w2"] = blocks(i["L0_ffn_rW1"]), blocks(i["L0_ffn_rW2"])
    a["r_b2"] = i["L0_ffn_rb2"].reshape(1, NE)
    a["e_w1"] = np.stack([blocks(w) for w in i["L0_ffn_We1"]], axis=1)
    a["e_w2"] = np.stack([blocks(w) for w in i["L0_ffn_We2"]], axis=1)
    a["e_b2"] = i["L0_ffn_be2"]
    a["wqkv"] = np.stack([blocks(i["L1_attn_W" + n].T) for n in "qkv"], axis=1)
    wx = np.zeros((4, D, C3, NH), np.float32)
    xcols = np.zeros((4, C3, NH), np.float32)
    for j, (n, rot) in enumerate((("v", 2), ("k", 1), ("v", 1), ("k", 2))):
        for comp in range(C3):
            row = (comp + rot) % C3
            for hd in range(NH):
                wx[j, hd * HD:(hd + 1) * HD, comp, hd] = i[f"L1_attn_W{n}s"][row]
                xcols[j, comp, hd] = i[f"L1_attn_b{n}s"][row]
    a["wx"] = np.stack([blocks(w.reshape(D, CX)) for w in wx], axis=1)
    a["xcols"] = xcols.reshape(4, CX).T
    wqs = np.zeros((C3, NH, D), np.float32)
    bqs = np.zeros((C3, NH, NH), np.float32)
    for hd in range(NH):
        for comp in range(C3):
            wqs[comp, hd, hd * HD:(hd + 1) * HD] = i["L1_attn_Wqs"][comp]
            bqs[comp, hd, hd] = i["L1_attn_bqs"][comp]
    a["wqs"], a["bqs"] = wqs.reshape(CX, D), bqs.reshape(CX, NH)
    a["temp"] = i["L1_attn_temp"].reshape(1, 1)
    a["fold"] = np.tile(np.eye(VW, dtype=np.float32), (P // VW, 1))
    a["wo"] = blocks(i["L1_attn_Wo"].T)
    a["w1"], a["w2"] = blocks(i["L1_ffn_W1"]), blocks(i["L1_ffn_W2"])
    a["b1"] = column(i["L1_ffn_b1"])
    a["bo"], a["b2"] = i["L1_attn_bo"].reshape(1, D), i["L1_ffn_b2"].reshape(1, D)
    return {n: np.ascontiguousarray(w) for n, w in a.items()}


SCRATCH = {"x2": ([TOK, D], F32), "v": ([TOK, D], F32), "q": ([B * D, CB, 3, CH], BF16),
           "k": ([B * D, CB, 3, CH], BF16), "kb": ([HEADS, CB, 3, CH], BF16),
           "neg": ([ROT, 2, L], BF16)}


def kernel(**inputs):
    import concourse.bacc as bacc
    from concourse.bass_utils import run_bass_kernel_spmd

    nc = bacc.Bacc("TRN2", target_bir_lowering=False, num_devices=1)
    arrays = lay_out({n: np.asarray(w) for n, w in inputs.items()})
    arrays = {"in_" + n: w for n, w in arrays.items()}
    a = {n[3:]: nc.dram_tensor(n, w.shape, mybir.dt.from_np(w.dtype), kind="ExternalInput").ap()
         for n, w in arrays.items()}
    out = nc.dram_tensor("out_y", [TOK, D], F32, kind="ExternalOutput").ap()
    scr = {n: nc.dram_tensor("scratch_" + n, shape, dt).ap() for n, (shape, dt) in SCRATCH.items()}
    mamba_moe_qkv(nc, a, scr)
    attention_ffn(nc, a, scr, out)
    r = run_bass_kernel_spmd(nc, [arrays], core_ids=[0])
    return r.results[0]["out_y"].reshape(B, L, D)
```
